# Optimizing a Trainium2 kernel written in Bass

```python
import numpy as np
import jax
import jax.numpy as jnp

def _softmax(x, axis=-1):
    return jax.nn.softmax(x, axis=axis)

def _gelu(x):
    return jax.nn.gelu(x, approximate=True)

def _silu(x):
    return jax.nn.silu(x)

def _sigmoid(x):
    return jax.nn.sigmoid(x)

def _layernorm(x, axis=-1, eps=1e-05):
    m = jnp.mean(x, axis=axis, keepdims=True)
    v = jnp.var(x, axis=axis, keepdims=True)
    return (x - m) / jnp.sqrt(v + eps)

def _scatter_add(tgt, idx, src, axis=0):
    return tgt.at[idx].add(src)

def _segment_sum(src, seg, n):
    return jax.ops.segment_sum(src, seg, n)
kernel_name = 'mk_hybrid_d1_jaxref_r8_8d0e67'

def setup_inputs(seed: int=0):
    np.random.seed(seed)
    _w = jnp.asarray

    def _L0_attn_a_setup():
        import math
        import jax, jax.numpy as jnp
        import numpy as np
        B, T, C = (2, 256, 256)
        H, G = (16, 4)
        D = C // H
        KV = G * D
        SOFT_CAP = 50.0
        EPS = 1e-06

        def _rmsnorm(x, w):
            rms = jnp.linalg.norm(x, axis=-1, keepdims=True) / math.sqrt(x.shape[-1])
            return w * (x / (rms + EPS))

        def _rotary_tables(seq_len, dim):
            inv_freq = 1.0 / 10000.0 ** (jnp.arange(0, dim, 2, dtype=jnp.float32) / dim)
            t = jnp.arange(seq_len, dtype=jnp.float32)
            freqs = jnp.outer(t, inv_freq)
            return (jnp.cos(freqs), jnp.sin(freqs))

        def _apply_rope(x, cos, sin):
            d = x.shape[-1] // 2
            x1, x2 = (x[..., :d], x[..., d:])
            c = cos[None, :, None, :]
            s = sin[None, :, None, :]
            return jnp.concatenate([x1 * c + x2 * s, -x1 * s + x2 * c], axis=-1)
        key = jax.random.key(seed)
        ks = jax.random.split(key, 5)
        s = 1.0 / math.sqrt(C)
        return {'x': jax.random.normal(ks[0], (B, T, C), jnp.float32), 'Wq': jax.random.normal(ks[1], (C, C), jnp.float32) * s, 'Wk': jax.random.normal(ks[2], (KV, C), jnp.float32) * s, 'Wv': jax.random.normal(ks[3], (KV, C), jnp.float32) * s, 'Wo': jax.random.normal(ks[4], (C, C), jnp.float32) * s, 'bo': jnp.zeros((C,), jnp.float32), 'q_norm_w': jnp.ones((D,), jnp.float32), 'k_norm_w': jnp.ones((D,), jnp.float32)}
    _L0_attn_a_in = _L0_attn_a_setup()

    def _L0_attn_b_setup():
        import jax, jax.numpy as jnp
        import numpy as np
        C = 8.0
        B, S, D = (4, 512, 256)
        key = jax.random.key(seed)
        k1, k2, k3, k4 = jax.random.split(key, 4)
        x = jax.random.normal(k1, (B, S, D), dtype=jnp.float32)
        std = 1.0 / np.sqrt(D)
        Wa = jax.random.normal(k2, (D, D), dtype=jnp.float32) * std
        Wx = jax.random.normal(k3, (D, D), dtype=jnp.float32) * std
        ba = jnp.zeros((D,), dtype=jnp.float32)
        bx = jnp.zeros((D,), dtype=jnp.float32)
        u = jax.random.uniform(k4, (D,), minval=0.9, maxval=0.999, dtype=jnp.float32)
        Lam = -jnp.log(u ** (-1.0 / C) - 1.0)
        return {'x': x, 'Wa': Wa, 'Wx': Wx, 'ba': ba, 'bx': bx, 'Lam': Lam}
    _L0_attn_b_in = _L0_attn_b_setup()

    def _L0_ffn_setup():
        import jax, jax.numpy as jnp
        import numpy as np
        TOP_K = 6
        N_GROUP = 8
        TOPK_GROUP = 3
        CAPACITY = 96
        RSF = 1.0
        key = jax.random.key(seed)
        ks = jax.random.split(key, 8)
        B, S, H = (1, 512, 256)
        E, M = (64, 176)
        MS = 352
        sc = 0.02
        return {'hidden_states': jax.random.normal(ks[0], (B, S, H), jnp.float32), 'gate_weight': jax.random.normal(ks[1], (E, H), jnp.float32) * sc, 'Wg': jax.random.normal(ks[2], (E, M, H), jnp.float32) * sc, 'Wu': jax.random.normal(ks[3], (E, M, H), jnp.float32) * sc, 'Wd': jax.random.normal(ks[4], (E, H, M), jnp.float32) * sc, 'Sg': jax.random.normal(ks[5], (MS, H), jnp.float32) * sc, 'Su': jax.random.normal(ks[6], (MS, H), jnp.float32) * sc, 'Sd': jax.random.normal(ks[7], (H, MS), jnp.float32) * sc}
    _L0_ffn_in = _L0_ffn_setup()
    _d = {'L0_attn_a_x': _L0_attn_a_in['x'], 'L0_attn_a_Wq': _L0_attn_a_in['Wq'], 'L0_attn_a_Wk': _L0_attn_a_in['Wk'], 'L0_attn_a_Wv': _L0_attn_a_in['Wv'], 'L0_attn_a_Wo': _L0_attn_a_in['Wo'], 'L0_attn_a_bo': _L0_attn_a_in['bo'], 'L0_attn_a_q_norm_w': _L0_attn_a_in['q_norm_w'], 'L0_attn_a_k_norm_w': _L0_attn_a_in['k_norm_w'], 'L0_attn_b_Wa': _L0_attn_b_in['Wa'], 'L0_attn_b_Wx': _L0_attn_b_in['Wx'], 'L0_attn_b_ba': _L0_attn_b_in['ba'], 'L0_attn_b_bx': _L0_attn_b_in['bx'], 'L0_attn_b_Lam': _L0_attn_b_in['Lam'], 'L0_ffn_gate_weight': _L0_ffn_in['gate_weight'], 'L0_ffn_Wg': _L0_ffn_in['Wg'], 'L0_ffn_Wu': _L0_ffn_in['Wu'], 'L0_ffn_Wd': _L0_ffn_in['Wd'], 'L0_ffn_Sg': _L0_ffn_in['Sg'], 'L0_ffn_Su': _L0_ffn_in['Su'], 'L0_ffn_Sd': _L0_ffn_in['Sd']}
    _x0 = _d['L0_attn_a_x']
    _d['L0_attn_a_x'] = jax.random.normal(jax.random.fold_in(jax.random.key(seed), 1), (1, 2048, 256), dtype=_x0.dtype)
    del _x0
    return _d

def reference(L0_attn_a_x, L0_attn_a_Wq, L0_attn_a_Wk, L0_attn_a_Wv, L0_attn_a_Wo, L0_attn_a_bo, L0_attn_a_q_norm_w, L0_attn_a_k_norm_w, L0_attn_b_Wa, L0_attn_b_Wx, L0_attn_b_ba, L0_attn_b_bx, L0_attn_b_Lam, L0_ffn_gate_weight, L0_ffn_Wg, L0_ffn_Wu, L0_ffn_Wd, L0_ffn_Sg, L0_ffn_Su, L0_ffn_Sd):

    def _L0_attn_a_ref(x, Wq, Wk, Wv, Wo, bo, q_norm_w, k_norm_w):
        import math
        import jax, jax.numpy as jnp
        import numpy as np
        B, T, C = (2, 256, 256)
        H, G = (16, 4)
        D = C // H
        KV = G * D
        SOFT_CAP = 50.0
        EPS = 1e-06

        def _rmsnorm(x, w):
            rms = jnp.linalg.norm(x, axis=-1, keepdims=True) / math.sqrt(x.shape[-1])
            return w * (x / (rms + EPS))

        def _rotary_tables(seq_len, dim):
            inv_freq = 1.0 / 10000.0 ** (jnp.arange(0, dim, 2, dtype=jnp.float32) / dim)
            t = jnp.arange(seq_len, dtype=jnp.float32)
            freqs = jnp.outer(t, inv_freq)
            return (jnp.cos(freqs), jnp.sin(freqs))

        def _apply_rope(x, cos, sin):
            d = x.shape[-1] // 2
            x1, x2 = (x[..., :d], x[..., d:])
            c = cos[None, :, None, :]
            s = sin[None, :, None, :]
            return jnp.concatenate([x1 * c + x2 * s, -x1 * s + x2 * c], axis=-1)
        b, t, c = x.shape
        q = (x @ Wq.T).reshape(b, t, H, D)
        k = (x @ Wk.T).reshape(b, t, G, D)
        v = (x @ Wv.T).reshape(b, t, G, D)
        cos, sin = _rotary_tables(t, D)
        q = _apply_rope(_rmsnorm(q, q_norm_w), cos, sin)
        k = _apply_rope(_rmsnorm(k, k_norm_w), cos, sin)
        q = q.transpose(0, 2, 1, 3)
        k = jnp.repeat(k.transpose(0, 2, 1, 3), H // G, axis=1)
        v = jnp.repeat(v.transpose(0, 2, 1, 3), H // G, axis=1)
        att = jnp.einsum('bhqd,bhkd->bhqk', q, k) / math.sqrt(D)
        causal = jnp.tril(jnp.ones((t, t), bool))
        att = jnp.where(causal[None, None], att, -jnp.inf)
        att = SOFT_CAP * jnp.tanh(att / SOFT_CAP)
        att = jax.nn.softmax(att, axis=-1)
        y = jnp.einsum('bhqk,bhkd->bhqd', att, v)
        y = y.transpose(0, 2, 1, 3).reshape(b, t, c)
        return y @ Wo.T + bo

    def _L0_attn_b_ref(x, Wa, Wx, ba, bx, Lam):
        import jax, jax.numpy as jnp
        import numpy as np
        C = 8.0
        B, S, D = (4, 512, 256)
        r = jax.nn.sigmoid(jnp.einsum('bsd,hd->bsh', x, Wa) + ba)
        i = jax.nn.sigmoid(jnp.einsum('bsd,hd->bsh', x, Wx) + bx)
        log_a = -C * jax.nn.softplus(-Lam) * r
        a = jnp.exp(log_a)
        u = jnp.sqrt(1.0 - a ** 2) * (i * x)
        a_t = jnp.moveaxis(a, 1, 0)
        u_t = jnp.moveaxis(u, 1, 0)

        def step(h, au):
            at, ut = au
            h = at * h + ut
            return (h, h)
        h0 = jnp.zeros((x.shape[0], x.shape[2]), dtype=x.dtype)
        _, y = jax.lax.scan(step, h0, (a_t, u_t))
        return jnp.moveaxis(y, 0, 1)

    def _L0_ffn_ref(hidden_states, gate_weight, Wg, Wu, Wd, Sg, Su, Sd):
        import jax, jax.numpy as jnp
        import numpy as np
        TOP_K = 6
        N_GROUP = 8
        TOPK_GROUP = 3
        CAPACITY = 96
        RSF = 1.0
        B, S, H = hidden_states.shape
        E, M, _ = Wg.shape
        K, NG, TG, C = (TOP_K, N_GROUP, TOPK_GROUP, CAPACITY)
        x = hidden_states.reshape(-1, H)
        T = x.shape[0]
        logits = x.astype(jnp.float32) @ gate_weight.astype(jnp.float32).T
        scores = jax.nn.softmax(logits, axis=-1)
        group_scores = scores.reshape(T, NG, E // NG).max(axis=-1)
        _, gidx = jax.lax.top_k(group_scores, TG)
        gmask = jnp.zeros((T, NG), scores.dtype).at[jnp.arange(T)[:, None], gidx].set(1.0)
        smask = jnp.repeat(gmask, E // NG, axis=1)
        tmp_scores = jnp.where(smask > 0, scores, 0.0)
        topk_w, topk_i = jax.lax.top_k(tmp_scores, K)
        topk_w = topk_w * RSF
        flat = topk_i.reshape(-1)
        oh = jax.nn.one_hot(flat, E, dtype=jnp.int32)
        pos = jnp.sum(jnp.cumsum(oh, axis=0) * oh, axis=-1) - 1
        slot = flat * C + jnp.minimum(pos, C - 1)
        tok = jnp.arange(T * K) // K
        buf = jnp.zeros((E * C, H), x.dtype).at[slot].set(x[tok]).reshape(E, C, H)
        g = jnp.einsum('ech,emh->ecm', buf, Wg)
        u = jnp.einsum('ech,emh->ecm', buf, Wu)
        out = jnp.einsum('ecm,ehm->ech', jax.nn.silu(g) * u, Wd).reshape(E * C, H)
        yk = out[slot].reshape(T, K, H)
        y = jnp.sum(yk * topk_w[..., None].astype(yk.dtype), axis=1)
        shared = jax.nn.silu(x @ Sg.T) * (x @ Su.T) @ Sd.T
        return (y + shared).reshape(B, S, H)
    x = L0_attn_a_x
    x = x + _L0_attn_a_ref(_layernorm(x, axis=-1), L0_attn_a_Wq, L0_attn_a_Wk, L0_attn_a_Wv, L0_attn_a_Wo, L0_attn_a_bo, L0_attn_a_q_norm_w, L0_attn_a_k_norm_w)
    x = x + _L0_ffn_ref(_layernorm(x, axis=-1), L0_ffn_gate_weight, L0_ffn_Wg, L0_ffn_Wu, L0_ffn_Wd, L0_ffn_Sg, L0_ffn_Su, L0_ffn_Sd)
    x = x + _L0_attn_b_ref(_layernorm(x, axis=-1), L0_attn_b_Wa, L0_attn_b_Wx, L0_attn_b_ba, L0_attn_b_bx, L0_attn_b_Lam)
    x = x + _L0_ffn_ref(_layernorm(x, axis=-1), L0_ffn_gate_weight, L0_ffn_Wg, L0_ffn_Wu, L0_ffn_Wd, L0_ffn_Sg, L0_ffn_Su, L0_ffn_Sd)
    return x

_drawn_inputs = setup_inputs


def setup_inputs(seed=0):
    import zlib

    import numpy as np

    out = dict(_drawn_inputs(seed))
    spreads = {'L0_attn_a_bo': (0.0, 0.1),
     'L0_attn_a_q_norm_w': (1.0, 0.558),
     'L0_attn_a_k_norm_w': (1.0, 0.6),
     'L0_attn_b_ba': (0.0, 0.641),
     'L0_attn_b_bx': (0.0, 0.395)}
    factors = {'L0_ffn_gate_weight': 8.0, 'L0_ffn_Wg': 8.0, 'L0_ffn_Wu': 8.0, 'L0_ffn_Wd': 8.0}
    for name, (base, spread) in spreads.items():
        noise = np.random.default_rng([zlib.crc32(name.encode()), seed]).standard_normal(out[name].shape)
        drawn = base * np.exp(spread * noise) if base else spread * noise
        out[name] = jnp.asarray(drawn.astype(out[name].dtype))
    for name, factor in factors.items():
        out[name] = (out[name] * factor).astype(out[name].dtype)
    return out
```

```python
from contextlib import ExitStack

import numpy as np

import concourse.bass as bass
from concourse import mybir

F32 = mybir.dt.float32
BF16 = mybir.dt.bfloat16
U32 = mybir.dt.uint32
I32 = mybir.dt.int32
ALU = mybir.AluOpType
ACT = mybir.ActivationFunctionType
AX = mybir.AxisListType

P = 128
T, C = 2048, 256
NT = T // P
CT = 4
NC = NT // CT
CW = CT * P
CH = C // P
H, G, D = 16, 4, 16
HG = H // G
QK = H + G
NPART = 6
SOFT_CAP = 50.0
E, M, CAP, TOPK, NGRP, TOPG = 64, 176, 96, 6, 8, 3
MH = M // 2
MS = 352
SC = MS // MH
EU = 8
EH = 4
OVER = 8192.0
VW = 32
LN_EPS, RMS_EPS = 1e-5, 1e-6


def constants():
    p = np.arange(P)
    ident = np.eye(P)
    before = (p[:, None] < p[None, :]) * 1.0
    diag = np.where(p[:, None] > p[None, :], -1.0, 2.0)
    wide = np.zeros((P, 2 * P))
    wide[:, P] = 1.0
    den = np.zeros((P, P))
    for j in range(HG):
        den[VW * j + D, VW * j:VW * (j + 1)] = 1.0
    tail = np.where(p[:, None] > np.arange(NT)[None, :], np.exp(-SOFT_CAP), 0.0)
    tail[NT:] = 0.0
    iota = np.broadcast_to(np.arange(E), (P, E))
    tok = P * np.arange(NT)[None, :] + p[:, None] + 1.0
    parts = [ident, before, diag, wide, den, tail, iota, tok]
    at, where = 0, {}
    for name, a in zip(("ident", "before", "diag", "wide", "den", "tail", "iota", "tok"), parts):
        where[name] = (at, at + a.shape[1])
        at += a.shape[1]
    inv = 1.0 / 10000.0 ** (np.arange(0, D, 2, dtype=np.float32) / np.float32(D))
    freqs = np.outer(np.arange(T, dtype=np.float32), inv.astype(np.float32))
    cs = np.stack([np.cos(freqs), np.sin(freqs)], 1).astype(np.float32)
    cs = cs.reshape(NT, P, 2, D // 2).transpose(1, 2, 0, 3)
    return np.concatenate(parts, 1).astype(np.float32), where, np.ascontiguousarray(cs)


def hybrid_kernel(nc, x_d, wqkv_d, wo_d, bo_d, nw_d, gate_d, wgu_d, wd_d, sgu_d, sd_d, wab_d, bab_d,
                  const_d, cs_d, out_d, where):
    with ExitStack() as whole:
        def sem(name):
            return whole.enter_context(nc.semaphore(name))

        def keep(name, shape, dt=F32):
            return whole.enter_context(nc.sbuf_tensor(name, shape, dt))

        buf_d = nc.dram_tensor("expert_in", [E * CAP, C], F32).ap()
        res_d = nc.dram_tensor("expert_out", [E * CAP, C], F32).ap()
        xn_d = nc.dram_tensor("normed", [T, C], F32).ap()

        PS = whole.enter_context(nc.psum_tensor("PS", [P, 8, 512], F32))
        X = keep("X", [P, NT, C])
        xnT = keep("xnT", [P, CH, CW])
        st = keep("st", [P, CT, 6])
        mv = keep("mv", [P, CT, 2])
        ve = keep("ve", [P, CT])
        rstd = keep("rstd", [P, CT])
        nt = keep("nt", [P, CT])
        half = keep("half", [P, CT * QK])
        consts = keep("consts", [P, const_d.shape[1]])
        identb = keep("identb", [P, P], BF16)
        xn = [keep(f"xn{i}", [P, CT, C]) for i in range(2)]

        def const(name):
            return consts[:, where[name][0]:where[name][1]]

        x_loaded, c_loaded, w_loaded, bo_loaded = map(sem, ("x_loaded", "c_loaded", "w_loaded", "bo_loaded"))
        xn_ready = sem("xn_ready")
        xnT_psum, xnT_ready = map(sem, ("xnT_psum", "xnT_ready"))
        setup, presets = map(sem, ("setup", "presets"))

        def norm_chunk(dve, n, c, xn_buf, waits=()):
            for r in range(CT):
                dve.bn_stats(st[:, r, :], X[:, c * CT + r, :])
            dve.drain()
            for r in range(CT):
                dve.bn_aggr(mv[:, r, :], st[:, r, :])
            dve.drain()
            dve.tensor_scalar(ve[:], mv[:, :, 1], LN_EPS, None, ALU.add)
            dve.drain()
            dve.tensor_scalar(rstd[:].bitcast(I32), ve[:].bitcast(I32), -0.5, float(0x5F3759DF), ALU.mult, ALU.add)
            dve.drain()
            for _ in range(4):
                dve.tensor_tensor(nt[:], rstd[:], rstd[:], ALU.mult)
                dve.drain()
                dve.tensor_tensor(nt[:], nt[:], ve[:], ALU.mult)
                dve.drain()
                dve.tensor_scalar(nt[:], nt[:], -0.5, 1.5, ALU.mult, ALU.add)
                dve.drain()
                dve.tensor_tensor(rstd[:], rstd[:], nt[:], ALU.mult)
                dve.drain()
            for s, v in waits:
                dve.wait_ge(s, v)
            for r in range(CT):
                last = dve.tensor_scalar(xn_buf[:, r, :], X[:, c * CT + r, :], mv[:, r, 0:1], rstd[:, r:r + 1],
                                         ALU.subtract, ALU.mult)
            last.then_inc(xn_ready, 1)

        def transpose_chunk(pe, n, xn_buf):
            pe.wait_ge(xn_ready, n + 1)
            pe.wait_ge(xnT_ready, n + 1)
            for h in range(CH):
                for r in range(CT):
                    last = pe.transpose(PS[:, h, r * P:(r + 1) * P], xn_buf[:, r, h * P:(h + 1) * P], const("ident"))
            last.then_inc(xnT_psum, 1)

        def evacuate_chunk(act, n, waits=()):
            for s, v in waits:
                act.wait_ge(s, v)
            act.wait_ge(xnT_psum, n + 1 + 1)
            act.activation(xnT[:], PS[:, 0:2, :], ACT.Copy).then_inc(xnT_ready, 1)

        qkv_psum, qkv_copied, sums_psum, sums_ready = map(
            sem, ("qkv_psum", "qkv_copied", "sums_psum", "sums_ready"))
        squares_ready, rms_ready, parts_ready, qt_psum, qt_ready = map(
            sem, ("squares_ready", "rms_ready", "parts_ready", "qt_psum", "qt_ready"))
        scores_ready, tanh_done, diag_done, exp_done, probs_used = map(
            sem, ("scores_ready", "tanh_done", "diag_done", "exp_done", "probs_used"))
        vst_ready, av_copied, den_psum, y_ready, o_psum, x1_ready = map(
            sem, ("vst_ready", "av_copied", "den_psum", "y_ready", "o_psum", "x1_ready"))

        logits_psum, shifted_ready, exps_ready, sel_ready, place_psum, last_psum, routed = map(
            sem, ("logits_psum", "shifted_ready", "exps_ready", "sel_ready", "place_psum", "last_psum", "routed"))
        shared_psum, shared_tanh, shared_act, shared_out, shared_added = map(
            sem, ("shared_psum", "shared_tanh", "shared_act", "shared_out", "shared_added"))
        dispatched = [sem(f"dispatched{i}") for i in range(2)]
        last_index, last_rows, last_stored = map(sem, ("last_index", "last_rows", "last_stored"))
        w_ld = [sem(f"expert_weights{i}") for i in range(EU)]
        x_ld = [sem(f"expert_inputs{i}") for i in range(2)]
        xt_psum, xt_ready, gu_psum, gate_tanh, act_ready, down_psum, out_copied = map(
            sem, ("xt_psum", "xt_ready", "gu_psum", "gate_tanh", "act_ready", "down_psum", "out_copied"))
        out_rows = [sem(f"expert_rows{i}") for i in range(2)]
        gathered = [sem(f"gathered{i}") for i in range(CT)]
        combined = sem("combined")
        gates_psum, gates_tanh, decay_ready, square_ready, root_ready, input_ready, state_ready, state_psum, x3_ready = map(
            sem, ("gates_psum", "gates_tanh", "decay_ready", "square_ready", "root_ready", "input_ready", "state_ready",
                  "state_psum", "x3_ready"))
        lam_abs, lam_exp, zero_ready, weights2_loaded, out_stored = map(
            sem, ("lam_abs", "lam_exp", "zero_ready", "weights2_loaded", "out_stored"))

        with ExitStack() as ctx:
            def sb(name, shape, dt=F32):
                return ctx.enter_context(nc.sbuf_tensor(name, shape, dt))

            wqkv = sb("wqkv", [P, CH, (H + 2 * G) * D])
            wo = sb("wo", [P, G, C])
            nw = sb("nw", [P, 2, D])
            cs = sb("cs", [P, 2, NT, D // 2])
            rot = sb("rot", [P, 2, 2, NT, D])
            qk = sb("qk", [P, NT, QK, D])
            parts = sb("parts", [P, CT, QK, NPART, D], BF16)
            ra = sb("ra", [P, CT, QK, D])
            rb = sb("rb", [P, CT, QK, D])
            ss = sb("ss", [P, CT * QK])
            ri = sb("ri", [P, CT * QK])
            QT = sb("QT", [NPART * D, H, CW], BF16)
            KT = sb("KT", [NPART * D, G, T], BF16)
            V = sb("V", [P, G, NT + 1, VW])
            Vst = sb("Vst", [P, NT + 1, VW])
            PR = sb("PR", [P, 3, HG, CW])
            av = sb("av", [P, G, CW])
            rden = sb("rden", [P, CW])

            block = ctx.enter_context(nc.Block())

            @block.sync
            def _(sp):
                sp.dma_start(X[:], x_d.rearrange("(i p) c -> p i c", p=P)).then_inc(x_loaded, 16)
                sp.dma_start(consts[:], const_d).then_inc(c_loaded, 16)
                sp.dma_start(wqkv[:], wqkv_d).then_inc(w_loaded, 16)
                sp.dma_start(cs[:], cs_d).then_inc(w_loaded, 16)
                sp.dma_start(nw[:], nw_d).then_inc(w_loaded, 16)
                sp.wait_ge(presets, 3)
                for j in range(HG):
                    sp.dma_start(wo[VW * j:VW * j + D, :, :], wo_d[:, j, :, :]).then_inc(bo_loaded, 16)
                sp.dma_start(wo[D:D + 1, 0, :], bo_d).then_inc(bo_loaded, 16)

            @block.gpsimd
            def _(pool):
                pool.memset(half[:], 0.5).then_inc(setup, 1)
                pool.memset(wo[:], 0.0).then_inc(presets, 1)
                pool.memset(V[:], 0.0).then_inc(presets, 1)
                pool.wait_ge(presets, 2)
                pool.memset(V[:, :, 0:NT, D:D + 1], 1.0).then_inc(presets, 1)
                pool.wait_ge(setup, 1)

                def rms_chunk(c):
                    pool.wait_ge(squares_ready, c + 1)
                    pool.tensor_tensor(ri[:], ss[:], half[:], ALU.pow).then_inc(rms_ready, 1)

                step_base = 0
                for c in range(NC):
                    rms_chunk(c)
                    steps = CT * (c + 1)
                    with pool.Fori(0, G) as g:
                        if c == 0:
                            pool.wait_ge(sums_ready, 1)
                        pool.wait_ge(probs_used, g * steps + step_base + 1)
                        pool.tensor_copy(Vst[:], V[:, g, :, :]).then_inc(vst_ready, 1)
                    step_base += G * steps

            @block.tensor
            def _(pe):
                for s in (xnT_psum, qkv_psum, probs_used, shared_out, place_psum, last_psum, shared_psum, down_psum):
                    pe.sem_inc(s, 1)
                pe.wait_ge(c_loaded, 16)
                pe.wait_ge(w_loaded, 48)
                with pe.Fori(0, NC) as c:
                    transpose_chunk(pe, c, xn[0])
                    pe.wait_ge(xnT_ready, c + 1 + 1)
                    pe.wait_ge(qkv_copied, c + 1)
                    for r in range(CT):
                        for h in range(CH):
                            last = pe.matmul(PS[:, 2 + r, 0:(H + 2 * G) * D], xnT[:, h, r * P:(r + 1) * P], wqkv[:, h, :],
                                             start=(h == 0), stop=(h == CH - 1))
                        last.then_inc(qkv_psum, 1)
                pe.wait_ge(qkv_copied, NC + 1)
                for j in range(NT):
                    last = pe.matmul(PS[:, 0, 0:G * VW], consts[:, where["wide"][0] + P - j:where["wide"][0] + 2 * P - j],
                                     V[:, :, j, :], start=(j == 0), stop=(j == NT - 1))
                last.then_inc(sums_psum, 1)

                step_base = unit_base = 0
                for c in range(NC):
                    steps = CT * (c + 1)
                    pe.wait_ge(parts_ready, c + 1)
                    if c:
                        pe.wait_ge(x1_ready, c)
                    for a in range(QK // 2):
                        n = c * (QK // 2) + a
                        if a >= 4 or c:
                            pe.wait_ge(qt_ready, n - 3 if a >= 4 else n)
                        bank = PS[:, a % 4, :].bitcast(BF16)
                        for hh in range(2):
                            for r in range(CT):
                                last = pe.transpose(bank[0:NPART * D, hh * CW + r * P:hh * CW + (r + 1) * P],
                                                    parts[:, r, 2 * a + hh, :, :].rearrange("p s d -> p (s d)"), identb[:])
                        last.then_inc(qt_psum, 1)
                    pe.wait_ge(qt_ready, (c + 1) * (QK // 2))

                    with pe.Fori(0, G) as g:
                        sbase = step_base + g * steps
                        ubase = unit_base + g * (2 * steps)

                        def cols(s):
                            return max(0, s - CT * c) * P

                        def scores(s):
                            for pr in range(2):
                                u = 2 * s + pr
                                pe.wait_ge(tanh_done, ubase + (u - 2 if u >= 3 else 0) + 1)
                                for hh in range(2):
                                    last = pe.matmul(PS[:, 2 * (u % 3) + hh, cols(s):CW],
                                                     KT[:, g, s * P:(s + 1) * P],
                                                     QT[:, g * HG + 2 * pr + hh, cols(s):CW], start=True, stop=True)
                                last.then_inc(scores_ready, 1)

                        def values(s):
                            pe.wait_ge(exp_done, sbase + s + 1)
                            if s == 0:
                                pe.wait_ge(vst_ready, g + (c * G + 1))
                                pe.wait_ge(av_copied, g + c * G + 1)
                            for j in range(HG):
                                last = pe.matmul(PS[VW * j:VW * (j + 1), 6, cols(s):CW], Vst[:, s, :],
                                                 PR[:, s % 3, j, cols(s):CW], start=(s == 0), stop=(s == steps - 1),
                                                 tile_position=(0, VW * j), skip_group_check=True)
                            last.then_inc(probs_used, 1)

                        scores(0)
                        scores(1)
                        for s in range(2, steps):
                            scores(s)
                            values(s - 2)
                        values(steps - 2)
                        tail = const("tail")[:, CT * c:CT * (c + 1)].unsqueeze(2).to_broadcast([P, CT, P])
                        for j in range(HG):
                            pe.matmul(PS[VW * j:VW * (j + 1), 6, :], Vst[:, NT, :], tail, start=False, stop=False,
                                      tile_position=(0, VW * j), skip_group_check=True)
                        values(steps - 1)
                    step_base += G * steps
                    unit_base += 2 * G * steps

                    for g in range(G):
                        pe.wait_ge(av_copied, c * G + g + 1 + 1)
                        pe.matmul(PS[:, g, :], const("den"), av[:, g, :], start=True, stop=True).then_inc(den_psum, 1)
                    pe.wait_ge(y_ready, G * (c + 1))
                    if c == 0:
                        pe.wait_ge(bo_loaded, 80)
                    for r in range(CT):
                        for g in range(G):
                            last = pe.matmul(PS[:, 4 + r // 2, (r % 2) * C:(r % 2 + 1) * C], av[:, g, r * P:(r + 1) * P],
                                             wo[:, g, :], start=(g == 0), stop=(g == G - 1), skip_group_check=True)
                    last.then_inc(o_psum, 1)

            @block.scalar
            def _(act):
                for s in (xnT_ready, tanh_done, xt_ready, out_copied):
                    act.sem_inc(s, 1)
                act.preload_act_table(ACT.Exp)
                with act.Fori(0, NC) as c:
                    evacuate_chunk(act, c, [(qkv_psum, c * CT + 1)])

                step_base = unit_base = 0
                for c in range(NC):
                    steps = CT * (c + 1)
                    with act.Fori(0, G) as g:
                        sbase = step_base + g * steps
                        ubase = unit_base + g * (2 * steps)

                        def cols(s):
                            return max(0, s - CT * c) * P

                        def tanhs(s):
                            act.wait_ge(probs_used, sbase + max(0, s - 2) + 1)
                            for pr in range(2):
                                u = 2 * s + pr
                                act.wait_ge(scores_ready, ubase + u + 1)
                                act.activation(PR[:, s % 3, 2 * pr:2 * pr + 2, cols(s):CW],
                                               PS[:, 2 * (u % 3):2 * (u % 3) + 2, cols(s):CW], ACT.Tanh,
                                               scale=1.0 / (SOFT_CAP * D ** 0.5)).then_inc(tanh_done, 1)

                        def exps(s):
                            if s >= CT * c:
                                act.wait_ge(diag_done, g * CT + (c * G * CT + s - CT * c + 1))
                            act.wait_ge(tanh_done, ubase + 2 * s + 2 + 1)
                            act.activation(PR[:, s % 3, :, cols(s):CW], PR[:, s % 3, :, cols(s):CW], ACT.Exp,
                                           scale=SOFT_CAP).then_inc(exp_done, 1)

                        tanhs(0)
                        for s in range(1, steps):
                            tanhs(s)
                            exps(s - 1)
                        exps(steps - 1)
                    step_base += G * steps
                    unit_base += 2 * G * steps

            @block.vector
            def _(dve):
                for s in (qkv_copied, av_copied, routed, shared_act, act_ready, combined):
                    dve.sem_inc(s, 1)
                dve.wait_ge(c_loaded, 16)
                dve.tensor_copy(identb[:], const("ident"))
                dve.wait_ge(w_loaded, 48)
                hd = D // 2
                for q in range(2):
                    for half_, (kind, sign) in ((0, (0, 1.0)), (1, (0, 1.0)), (0, (1, 1.0)), (1, (1, -1.0))):
                        src = half_ if kind == 0 else 1 - half_
                        dve.scalar_tensor_tensor(rot[:, q, kind, :, half_ * hd:(half_ + 1) * hd], cs[:, kind, :, :], sign,
                                                 nw[:, q, src * hd:(src + 1) * hd].unsqueeze(1).to_broadcast([P, NT, hd]),
                                                 ALU.mult, ALU.mult)
                dve.wait_ge(x_loaded, 16)
                dve.wait_ge(presets, 3)
                with dve.Fori(0, NC) as c:
                    norm_chunk(dve, c, c, xn[0], [(xnT_psum, c + 1)])
                    for r in range(CT):
                        dve.wait_ge(qkv_psum, c * CT + (r + 1) + 1)
                        dve.tensor_copy(qk[:, c * CT + r, :, :],
                                        PS[:, 2 + r, 0:QK * D].rearrange("p (h d) -> p h d", h=QK))
                        last = dve.tensor_copy(V[:, :, c * CT + r, 0:D],
                                               PS[:, 2 + r, QK * D:(QK + G) * D].rearrange("p (g d) -> p g d", g=G))
                    last.then_inc(qkv_copied, 1)
                dve.wait_ge(sums_psum, 1)
                dve.tensor_copy(V[:, :, NT, :], PS[:, 0, 0:G * VW].rearrange("p (g d) -> p g d", g=G)).then_inc(sums_ready, 1)

                def rotate(c):
                    q = qk[:, CT * c:CT * (c + 1), :, :]
                    flat = q.rearrange("p r h d -> p (r h) d")
                    raf, rbf = (a[:].rearrange("p r h d -> p (r h) d") for a in (ra, rb))
                    dve.drain()
                    dve.tensor_tensor(raf, flat, flat, ALU.mult)
                    dve.drain()
                    dve.tensor_reduce(ss[:], raf, AX.X, ALU.add).then_inc(squares_ready, 1)
                    dve.wait_ge(rms_ready, c + 1)
                    dve.tensor_scalar(ri[:], ri[:], D ** -0.5, RMS_EPS, ALU.mult, ALU.add)
                    dve.drain()
                    dve.reciprocal(ri[:], ri[:])
                    dve.drain()
                    dve.tensor_tensor(flat, flat, ri[:].unsqueeze(2).to_broadcast([P, CT * QK, D]), ALU.mult)
                    dve.drain()
                    for which, h0, h1 in ((0, 0, H), (1, H, QK)):
                        def table(kind, d0, d1):
                            return rot[:, which, kind, CT * c:CT * (c + 1), d0:d1].unsqueeze(2).to_broadcast([P, CT, h1 - h0, d1 - d0])
                        dve.tensor_tensor(ra[:, :, h0:h1, :], q[:, :, h0:h1, :], table(0, 0, D), ALU.mult)
                        dve.tensor_tensor(rb[:, :, h0:h1, 0:hd], q[:, :, h0:h1, hd:D], table(1, 0, hd), ALU.mult)
                        dve.tensor_tensor(rb[:, :, h0:h1, hd:D], q[:, :, h0:h1, 0:hd], table(1, hd, D), ALU.mult)
                    dve.drain()
                    dve.tensor_tensor(raf, raf, rbf, ALU.add)
                    if c:
                        dve.wait_ge(qt_psum, c * (QK // 2))
                    dve.drain()

                    def slot(s, h0=0, h1=QK):
                        return parts[:, :, h0:h1, s, :]
                    dve.tensor_copy(slot(0), ra[:])
                    dve.drain()
                    dve.tensor_tensor(rb[:], ra[:], slot(0), ALU.subtract)
                    dve.tensor_copy(slot(1, 0, H), slot(0, 0, H))
                    dve.tensor_copy(slot(4, 0, H), slot(0, 0, H))
                    dve.tensor_copy(slot(2, H, QK), slot(0, H, QK))
                    dve.tensor_copy(slot(5, H, QK), slot(0, H, QK))
                    dve.drain()
                    dve.tensor_copy(slot(3), rb[:])
                    dve.drain()
                    dve.tensor_tensor(ra[:], rb[:], slot(3), ALU.subtract)
                    dve.tensor_copy(slot(2, 0, H), slot(3, 0, H))
                    dve.tensor_copy(slot(1, H, QK), slot(3, H, QK))
                    dve.drain()
                    dve.tensor_copy(slot(5, 0, H), ra[:, :, 0:H, :])
                    dve.tensor_copy(slot(4, H, QK), ra[:, :, H:QK, :]).then_inc(parts_ready, 1)

                def take_transposed(c):
                    for a in range(QK // 2):
                        dve.wait_ge(qt_psum, c * (QK // 2) + a + 1)
                        dst = QT[:, 2 * a:2 * a + 2, :] if a < H // 2 else KT[:, 2 * a - H:2 * a - H + 2, CW * c:CW * (c + 1)]
                        dve.tensor_copy(dst, PS[0:NPART * D, a % 4, :].bitcast(BF16).rearrange("p (a n) -> p a n", a=2))\
                           .then_inc(qt_ready, 1)

                step_base = unit_base = 0
                rotate(0)
                for c in range(NC):
                    steps = CT * (c + 1)
                    take_transposed(c)

                    def head_group(g):
                        for r in range(CT):
                            s = CT * c + r
                            dve.wait_ge(tanh_done, unit_base + g * (2 * steps) + 2 * s + 2 + 1)
                            blk = PR[:, s % 3, :, r * P:(r + 1) * P]
                            dve.tensor_tensor(blk, blk, const("diag").unsqueeze(1).to_broadcast([P, HG, P]), ALU.min)\
                               .then_inc(diag_done, 1)
                        dve.wait_ge(probs_used, g * steps + (step_base + steps) + 1)
                        if c:
                            dve.wait_ge(o_psum, c)
                        dve.tensor_copy(av[:, g, :], PS[:, 6, :]).then_inc(av_copied, 1)

                    with dve.Fori(0, G - 1) as g:
                        head_group(g)
                    if 0 < c < NC - 1:
                        rotate(c + 1)
                    head_group(G - 1)
                    if c == 0:
                        rotate(1)
                    step_base += G * steps
                    unit_base += 2 * G * steps
                    for g in range(G):
                        dve.wait_ge(den_psum, c * G + g + 1)
                        dve.reciprocal(rden[:], PS[:, g, :])
                        dve.drain()
                        dve.tensor_tensor(av[:, g, :], av[:, g, :], rden[:], ALU.mult).then_inc(y_ready, 1)
                        dve.drain()
                    dve.wait_ge(o_psum, c + 1)
                    xc = X[:, CT * c:CT * (c + 1), :].rearrange("p r n -> p (r n)")
                    dve.tensor_tensor(xc, xc, PS[:, 4:6, :].rearrange("p b n -> p (b n)"), ALU.add).then_inc(x1_ready, 1)
        wgate = keep("wgate", [P, CH, E])
        sgu = keep("sgu", [P, CH, 2 * MS])
        sd = keep("sd", [MH, SC, C])
        wab = keep("wab", [P, CH, 2 * C])
        bab = keep("bab", [P, 3, CH])
        WGU = keep("WGU", [P, EU, CH, 2 * M])
        WD = keep("WD", [MH, EU, 2, C])
        XE = keep("XE", [CAP, 2, EH, C])
        XT = keep("XT", [P, 2, EH, CH, CAP])
        gth = keep("gth", [MH, 2, 2 * CAP])
        gta = keep("gta", [MH, 2 * CAP])
        ha = keep("ha", [MH, 2, 2, CAP])
        ob = keep("ob", [CAP, 2, EH, C])
        GB = keep("GB", [P, CT, TOPK, C])
        tri = keep("tri", [P, P], BF16)
        onesb = keep("onesb", [P, P], BF16)
        lsh = keep("lsh", [P, CT, E])
        red = keep("red", [P, CT])
        gs = keep("gs", [P, CT, NGRP])
        g8 = keep("g8", [P, CT, 8])
        gi = keep("gi", [P, CT, 8], U32)
        gif = keep("gif", [P, CT, 8])
        gc = keep("gc", [P, CT, TOPG, NGRP])
        w8 = keep("w8", [P, CT, 8])
        ei = keep("ei", [P, CT, 8], U32)
        eif = keep("eif", [P, CT, 8])
        OH = keep("OH", [P, CT, TOPK, E])
        sel = keep("sel", [P, CT, E])
        selb = keep("selb", [P, CT, E], BF16)
        selt = keep("selt", [P, CT, E])
        slot = keep("slot", [P, CT, E])
        over = keep("over", [P, CT, E])
        sl = [keep(f"sl{i}", [P, CT, TOPK]) for i in range(2)]
        sc_ = keep("sc_", [P, CT, TOPK])
        slf = keep("slf", [P, CT, TOPK])
        eb = [keep(f"eb{i}", [P, CT, TOPK]) for i in range(2)]
        run = keep("run", [P, E])
        runlast = keep("runlast", [E, 2])
        lidx = keep("lidx", [E, 1], U32)
        lrow = keep("lrow", [E, C])
        didx = [keep(f"didx{i}", [P, CT, TOPK], U32) for i in range(2)]
        cst = keep("cst", [P, CT, TOPK], U32)
        CIDX = keep("CIDX", [P, NT, TOPK], U32)
        WK = keep("WK", [P, NT, TOPK])
        sth = keep("sth", [MH, 2, CW])
        sta = keep("sta", [MH, CW])
        sact = keep("sact", [MH, SC, CW])
        zero = keep("zero", [P, C])
        xr = keep("xr", [P, CT, C])
        ra_ = keep("ra_", [P, CH, CW])
        ia_ = keep("ia_", [P, CH, CW])
        qa_ = keep("qa_", [P, CH, CW])
        hT = keep("hT", [P, CH, CW])
        hc = keep("hc", [P, CH])
        lam = keep("lam", [P, 8, CH])

        buf_e = buf_d.rearrange("(e s) c -> s e c", s=CAP)
        res_e = res_d.rearrange("(e s) c -> s e c", s=CAP)
        block = whole.enter_context(nc.Block())

        def n_pre(f, c):
            return c + NC if f == 0 else c * 2 + (2 * NC + 1)

        def n_rec(c):
            return c * 2 + 2 * NC

        @block.sync
        def _(sp):
            for dst, src in ((wgate, gate_d), (sgu, sgu_d), (sd, sd_d), (wab, wab_d), (bab, bab_d)):
                sp.dma_start(dst[:], src).then_inc(weights2_loaded, 16)

            def weights(t, e0, q, wait=True):
                if wait:
                    sp.wait_ge(down_psum, t * EU + (q + 1 - EU) + 1)
                sp.dma_start(WGU[:, q, :, :], wgu_d[bass.ds(e0 + q, 1), :, :, :].rearrange("e p h m -> p (e h m)")).then_inc(w_ld[q], 16)
                sp.dma_start(WD[:, q, :, :], wd_d[bass.ds(e0 + q, 1), :, :, :].rearrange("e p h m -> p (e h m)")).then_inc(w_ld[q], 16)

            def inputs(t, e0, hf, wait=True):
                if wait:
                    sp.wait_ge(xt_psum, t * 2 + (hf - 1))
                sp.dma_start(XE[:, hf, :, :], buf_e[:, bass.ds(e0 + EH * hf, EH), :]).then_inc(x_ld[hf], 16)

            turns = E // EU
            for f in range(2):
                for q in range(EU):
                    weights(turns * f, 0, q, wait=f > 0)
                for par in range(2):
                    sp.wait_ge(dispatched[par], 16 + 16 * (CT * TOPK + 1) * (NC // 2) * (f + 1))
                sp.wait_ge(last_stored, 16 * (f + 1))
                for hf in range(2):
                    inputs(turns * f, 0, hf, wait=f > 0)
                with sp.Fori(1, turns) as ee:
                    t = ee + turns * f
                    for q in range(EU):
                        weights(t, ee * EU, q)
                        if q % EH == EH - 1:
                            inputs(t, ee * EU, q // EH)
            with sp.Fori(0, NC) as c:
                sp.wait_ge(combined, c * CT + (NT + CT) + 1)
                sp.dma_start(out_d.rearrange("(i p) c -> p i c", p=P)[:, bass.ds(c * CT, CT), :],
                             X[:, bass.ds(c * CT, CT), :]).then_inc(out_stored, 16)
            sp.wait_ge(out_stored, 16 * NC)

        @block.gpsimd
        def _(pool):
            pool.memset(zero[:], 0.0).then_inc(zero_ready, 1)
            pool.wait_ge(zero_ready, 1)
            quarter = E * CAP // 4
            for i, s in enumerate((dispatched[0], dispatched[1], out_rows[0], out_rows[1])):
                pool.dma_start(buf_d[i * quarter:(i + 1) * quarter, :].rearrange("(p a) c -> p a c", p=P),
                               zero[:].unsqueeze(1).to_broadcast([P, quarter // P, C])).then_inc(s, 16)
            for s in dispatched + out_rows:
                pool.wait_ge(s, 16)

            def dispatch(f, c, par):
                pool.wait_ge(xn_ready, n_pre(f, c) + 1)
                pool.dma_start(xn_d.rearrange("(i p) c -> p i c", p=P)[:, bass.ds(c * CT, CT), :], xn[par][:])\
                    .then_inc(dispatched[par], 16)
                pool.wait_ge(dispatched[par], 16)
                pool.wait_ge(routed, c + (NC * f + 1) + 1)
                pool.tensor_tensor(slf[:], sl[par][:], eb[par][:], ALU.add)
                pool.drain()
                pool.tensor_copy(didx[par][:], slf[:])
                pool.drain()
                for r in range(CT):
                    for k in range(TOPK):
                        pool.indirect_dma_start(
                            out=buf_d, out_offset=bass.IndirectOffsetOnAxis(ap=didx[par][:, r, k:k + 1], axis=0),
                            in_=xn[par][:, r, :], in_offset=None, bounds_check=E * CAP - 1, oob_is_err=False)\
                            .then_inc(dispatched[par], 16)

            def last_slot(f):
                for par in range(2):
                    pool.wait_ge(dispatched[par], 16 + 16 * (CT * TOPK + 1) * (NC // 2) * (f + 1))
                pool.wait_ge(last_index, f + 1)
                pool.indirect_dma_start(out=lrow[:], out_offset=None, in_=xn_d,
                                        in_offset=bass.IndirectOffsetOnAxis(ap=lidx[:], axis=0),
                                        bounds_check=T - 1, oob_is_err=False).then_inc(last_rows, 16)
                pool.wait_ge(last_rows, 16 * (f + 1))
                pool.dma_start(buf_d.rearrange("(e s) c -> e s c", s=CAP)[:, CAP - 1, :], lrow[:]).then_inc(last_stored, 16)

            def store_rows(f):
                with pool.Fori(0, E // EU) as ee:
                    for hf in range(2):
                        pool.wait_ge(out_copied, ee * EU + (E * f + EH * (hf + 1)) + 1)
                        pool.dma_start(res_e[:, bass.ds(ee * EU + EH * hf, EH), :], ob[:, hf, :, :]).then_inc(out_rows[hf], 16)
                for hf in range(2):
                    pool.wait_ge(out_rows[hf], 16 * (E // EU * (f + 1) + 1))

            def gather(f, c):
                pool.wait_ge(combined, c * CT + NT * f + 1)
                pool.tensor_copy(cst[:], CIDX[:, bass.ds(c * CT, CT), :])
                pool.drain()
                for r in range(CT):
                    for k in range(TOPK):
                        pool.indirect_dma_start(out=GB[:, r, k, :], out_offset=None, in_=res_d,
                                                in_offset=bass.IndirectOffsetOnAxis(ap=cst[:, r, k:k + 1], axis=0),
                                                bounds_check=E * CAP - 1, oob_is_err=False).then_inc(gathered[r], 16)

            with pool.Fori(0, NC // 2) as cc:
                for par in range(2):
                    c = cc * 2 + par
                    dispatch(0, c, par)
            last_slot(0)
            store_rows(0)
            gather(0, 0)
            for c in range(NC):
                if c < NC - 1:
                    gather(0, c + 1)
                dispatch(1, c, c % 2)
            last_slot(1)
            store_rows(1)
            with pool.Fori(0, NC) as c:
                gather(1, c)

        @block.tensor
        def _(pe):
            pe.wait_ge(weights2_loaded, 80)

            def route(f, c, par):
                k = c + NC * f
                n = n_pre(f, c)
                transpose_chunk(pe, n, xn[par])
                pe.wait_ge(xnT_ready, n + 1 + 1)
                pe.wait_ge(routed, k + 1)
                for r in range(CT):
                    for h in range(CH):
                        last = pe.matmul(PS[:, 2, r * E:(r + 1) * E], xnT[:, h, r * P:(r + 1) * P], wgate[:, h, :],
                                         start=(h == 0), stop=(h == CH - 1))
                last.then_inc(logits_psum, 1)
                for m in range(SC):
                    pe.wait_ge(shared_act, k * SC + max(0, m - 1) + 1)
                    for j in range(2):
                        for h in range(CH):
                            last = pe.matmul(PS[0:MH, 3 + 2 * (m % 2) + j, :], sgu[:, h, MS * j + MH * m:MS * j + MH * (m + 1)],
                                             xnT[:, h, :], start=(h == 0), stop=(h == CH - 1))
                    last.then_inc(shared_psum, 1)
                pe.wait_ge(shared_act, k * SC + SC + 1)
                for r in range(CT):
                    for m in range(SC):
                        last = pe.matmul(PS[:, 7 if r < 2 else 3, (r % 2) * C:(r % 2 + 1) * C], sact[:, m, r * P:(r + 1) * P],
                                         sd[:, m, :], start=(m == 0), stop=(m == SC - 1), skip_group_check=True)
                last.then_inc(shared_out, 1)
                pe.wait_ge(sel_ready, k + 1)
                for r in range(CT):
                    for j in range(r + 1):
                        pe.matmul(PS[:, 4, r * E:(r + 1) * E], onesb[:] if j < r else tri[:], selb[:, j, :],
                                  start=(j == 0), stop=(j == r), skip_group_check=True)
                for j in range(CT):
                    last = pe.matmul(PS[:, 4, CT * E:(CT + 1) * E], onesb[:], selb[:, j, :], start=(j == 0), stop=(j == CT - 1),
                                     skip_group_check=True)
                last.then_inc(place_psum, 1)
                for r in range(CT):
                    last = pe.transpose(PS[0:E, 5, r * P:(r + 1) * P], selt[:, r, :], const("ident"))
                last.then_inc(last_psum, 1)

            def experts(f):
                pe.wait_ge(routed, NC * (f + 1) + 1)
                with pe.Fori(0, E // EU) as ee:
                    t = ee + (E // EU) * f
                    K = ee * EU + E * f

                    def turn(hf):
                        pe.wait_ge(x_ld[hf], t * 16 + 16)
                        pe.wait_ge(xt_ready, t * 2 + hf + 1)
                        for j in range(EH):
                            for h in range(CH):
                                last = pe.transpose(PS[:, 2 * hf + j // 2, ((j % 2) * CH + h) * CAP:((j % 2) * CH + h + 1) * CAP],
                                                    XE[:, hf, j, h * P:(h + 1) * P], const("ident")[0:CAP, 0:CAP])
                        last.then_inc(xt_psum, 1)

                    def gate_up(q):
                        pe.wait_ge(w_ld[q], t * 32 + 32)
                        pe.wait_ge(xt_ready, t * 2 + (q // EH + 1) + 1)
                        pe.wait_ge(act_ready, K + max(0, q - 1) + 1)
                        for j in range(4):
                            for h in range(CH):
                                last = pe.matmul(PS[0:MH, 4 + q % 2, j * CAP:(j + 1) * CAP], WGU[:, q, h, MH * j:MH * (j + 1)],
                                                 XT[:, q // EH, q % EH, h, :], start=(h == 0), stop=(h == CH - 1))
                        last.then_inc(gu_psum, 1)

                    def down(q):
                        pe.wait_ge(act_ready, K + q + 1 + 1)
                        pe.wait_ge(out_copied, K + max(0, q - 1) + 1)
                        for m in range(2):
                            last = pe.matmul(PS[0:CAP, 6 + q % 2, 0:C], ha[:, q % 2, m, :], WD[:, q, m, :],
                                             start=(m == 0), stop=(m == 1))
                        last.then_inc(down_psum, 1)

                    turn(0)
                    for q in range(EU):
                        gate_up(q)
                        if q == EH - 1:
                            turn(1)
                        if q:
                            down(q - 1)
                    down(EU - 1)

            def recur(c):
                n = n_rec(c)
                transpose_chunk(pe, n, xr)
                pe.wait_ge(xnT_ready, n + 1 + 1)
                pe.wait_ge(routed, c + NC + 1)
                for j in range(4):
                    for h in range(CH):
                        last = pe.matmul(PS[:, 2 + j, :], wab[:, h, P * j:P * (j + 1)], xnT[:, h, :],
                                         start=(h == 0), stop=(h == CH - 1))
                last.then_inc(gates_psum, 1)
                pe.wait_ge(state_ready, c + 1)
                for r in range(CT):
                    for h in range(CH):
                        last = pe.transpose(PS[:, 6 + r // 2, (r % 2) * C + h * P:(r % 2) * C + (h + 1) * P],
                                            hT[:, h, r * P:(r + 1) * P], const("ident"))
                last.then_inc(state_psum, 1)

            with pe.Fori(0, NC // 2) as cc:
                for par in range(2):
                    route(0, cc * 2 + par, par)
            experts(0)
            with pe.Fori(0, NC // 2) as cc:
                for par in range(2):
                    recur(cc * 2 + par)
                    route(1, cc * 2 + par, par)
            experts(1)

        @block.scalar
        def _(act):
            act.wait_ge(lam_abs, 1)
            act.activation(lam[:, 1, :], lam[:, 0, :], ACT.Exp, scale=-1.0).then_inc(lam_exp, 1)

            def route(f, c):
                k = c + NC * f
                n = n_pre(f, c)
                evacuate_chunk(act, n, [(shared_psum, k * SC + 1)] if f == 0 else [(input_ready, c + 1)])
                for m in range(SC):
                    act.wait_ge(shared_psum, k * SC + (m + 1) + 1)
                    act.wait_ge(shared_act, k * SC + max(0, m - 1) + 1)
                    act.activation(sth[:, m % 2, :], PS[0:MH, 3 + 2 * (m % 2), :], ACT.Tanh, scale=0.5).then_inc(shared_tanh, 1)
                    if m == 0:
                        act.wait_ge(shifted_ready, k + 1)
                        act.activation(lsh[:], lsh[:], ACT.Exp).then_inc(exps_ready, 1)

            def experts(f):
                with act.Fori(0, E // EU) as ee:
                    t = ee + (E // EU) * f
                    K = ee * EU + E * f

                    def turned(hf):
                        act.wait_ge(xt_psum, t * 2 + (hf + 1))
                        for i in range(2):
                            last = act.activation(XT[:, hf, 2 * i:2 * i + 2, :, :].rearrange("p a h s -> p (a h s)"),
                                                  PS[:, 2 * hf + i, 0:4 * CAP], ACT.Copy)
                        last.then_inc(xt_ready, 1)

                    def gate(q):
                        act.wait_ge(gu_psum, K + q + 1)
                        act.wait_ge(act_ready, K + max(0, q - 1) + 1)
                        act.activation(gth[:, q % 2, :], PS[0:MH, 4 + q % 2, 0:2 * CAP], ACT.Tanh, scale=0.5).then_inc(gate_tanh, 1)

                    def out(q):
                        if q % EH == 0:
                            act.wait_ge(out_rows[q // EH], t * 16 + 16)
                        act.wait_ge(down_psum, K + q + 1 + 1)
                        act.activation(ob[:, q // EH, q % EH, :], PS[0:CAP, 6 + q % 2, 0:C], ACT.Copy).then_inc(out_copied, 1)

                    turned(0)
                    for q in range(EU):
                        gate(q)
                        if q == EH - 1:
                            turned(1)
                        if q:
                            out(q - 1)
                    out(EU - 1)

            def recur(c):
                n = n_rec(c)
                evacuate_chunk(act, n, [(shared_psum, c * SC + NC * SC + 1)])
                act.wait_ge(gates_psum, c + 1)
                for j in range(4):
                    dst = (ra_ if j < 2 else ia_)[:, j % 2, :]
                    last = act.activation(dst, PS[:, 2 + j, :], ACT.Tanh, scale=0.5, bias=lam[:, 4 + j // 2, j % 2:j % 2 + 1])
                last.then_inc(gates_tanh, 1)
                act.wait_ge(gates_tanh, c + 1)
                for h in range(CH):
                    last = act.activation(ra_[:, h, :], ra_[:, h, :], ACT.Exp, scale=lam[:, 6, h:h + 1], bias=lam[:, 6, h:h + 1])
                last.then_inc(decay_ready, 1)
                act.wait_ge(square_ready, c + 1)
                act.activation(qa_[:], qa_[:], ACT.Sqrt, scale=-1.0, bias=1.0).then_inc(root_ready, 1)

            with act.Fori(0, NC // 2) as cc:
                for par in range(2):
                    route(0, cc * 2 + par)
            act.preload_act_table(ACT.Exp)
            experts(0)
            with act.Fori(0, NC // 2) as cc:
                for par in range(2):
                    recur(cc * 2 + par)
                    route(1, cc * 2 + par)
            act.preload_act_table(ACT.Exp)
            experts(1)

        @block.vector
        def _(dve):
            dve.tensor_copy(tri[:], const("before"))
            dve.memset(onesb[:], 1.0)
            dve.memset(hc[:], 0.0)
            dve.wait_ge(weights2_loaded, 80)
            L = bab[:, 2, :]
            dve.scalar_tensor_tensor(lam[:, 0, :], L, -1.0, L, ALU.mult, ALU.max).then_inc(lam_abs, 1)
            dve.tensor_scalar(lam[:, 4, :], bab[:, 0, :], 0.5, None, ALU.mult)
            dve.tensor_scalar(lam[:, 5, :], bab[:, 1, :], 0.5, None, ALU.mult)
            dve.wait_ge(lam_exp, 1)
            chain = [lambda: dve.tensor_scalar(lam[:, 2, :], lam[:, 1, :], 2.0, None, ALU.add),
                     lambda: dve.reciprocal(lam[:, 2, :], lam[:, 2, :]),
                     lambda: dve.tensor_tensor(lam[:, 1, :], lam[:, 1, :], lam[:, 2, :], ALU.mult),
                     lambda: dve.tensor_tensor(lam[:, 2, :], lam[:, 1, :], lam[:, 1, :], ALU.mult),
                     lambda: dve.tensor_scalar(lam[:, 3, :], lam[:, 2, :], 1 / 17, 1 / 15, ALU.mult, ALU.add)]
            for step in chain:
                step()
                dve.drain()
            for d in (13, 11, 9, 7, 5, 3, 1):
                dve.tensor_tensor(lam[:, 3, :], lam[:, 3, :], lam[:, 2, :], ALU.mult)
                dve.drain()
                dve.tensor_scalar(lam[:, 3, :], lam[:, 3, :], 1.0 / d, None, ALU.add)
                dve.drain()
            dve.scalar_tensor_tensor(lam[:, 1, :], lam[:, 1, :], 2.0, lam[:, 3, :], ALU.mult, ALU.mult)
            dve.tensor_scalar(lam[:, 2, :], L, -1.0, 0.0, ALU.mult, ALU.max)
            dve.drain()
            dve.tensor_tensor(lam[:, 1, :], lam[:, 1, :], lam[:, 2, :], ALU.add)
            dve.drain()
            dve.tensor_scalar(lam[:, 6, :], lam[:, 1, :], -4.0, None, ALU.mult)
            dve.drain()

            def bcast(ap, axis, shape):
                return ap.unsqueeze(axis).to_broadcast(shape)

            def route(f, c, par, cc):
                k = c + NC * f
                n = n_pre(f, c)
                norm_chunk(dve, n, c, xn[par], [(dispatched[par], cc * (16 * (CT * TOPK + 1)) + (16 + 16 * (CT * TOPK + 1) * (NC // 2) * f))])

                def shared(m):
                    if m == 0:
                        dve.drain()
                        dve.wait_ge(shared_out, k + 1)
                    dve.wait_ge(shared_tanh, k * SC + (m + 1))
                    dve.scalar_tensor_tensor(sta[:], sth[:, m % 2, :], 1.0, PS[0:MH, 3 + 2 * (m % 2), :], ALU.add, ALU.mult)
                    dve.drain()
                    dve.scalar_tensor_tensor(sact[:, m, :], PS[0:MH, 4 + 2 * (m % 2), :], 0.5, sta[:], ALU.mult, ALU.mult)\
                       .then_inc(shared_act, 1)

                dve.wait_ge(logits_psum, k + 1)
                lg = PS[:, 2, 0:CT * E].rearrange("p (r e) -> p r e", r=CT)
                dve.tensor_reduce(red[:], lg, AX.X, ALU.max)
                dve.drain()
                dve.tensor_tensor(lsh[:], lg, bcast(red[:], 2, [P, CT, E]), ALU.subtract).then_inc(shifted_ready, 1)
                shared(0)
                dve.drain()
                dve.wait_ge(exps_ready, k + 1)
                dve.tensor_reduce(red[:], lsh[:], AX.X, ALU.add)
                dve.drain()
                dve.reciprocal(red[:], red[:])
                dve.drain()
                dve.tensor_tensor(lsh[:], lsh[:], bcast(red[:], 2, [P, CT, E]), ALU.mult)
                dve.drain()
                dve.tensor_reduce(gs[:], lsh[:].rearrange("p r (g e) -> p r g e", g=NGRP), AX.X, ALU.max)
                dve.drain()
                for r in range(CT):
                    dve.max(g8[:, r, :], gs[:, r, :])
                dve.drain()
                for r in range(CT):
                    dve.max_index(gi[:, r, :], g8[:, r, :], gs[:, r, :])
                dve.drain()
                dve.tensor_copy(gif[:], gi[:])
                dve.drain()
                iota = const("iota")
                dve.tensor_tensor(gc[:], iota[:, 0:NGRP].unsqueeze(1).unsqueeze(1).to_broadcast([P, CT, TOPG, NGRP]),
                                  gif[:, :, 0:TOPG].unsqueeze(3).to_broadcast([P, CT, TOPG, NGRP]), ALU.is_equal)
                shared(1)
                dve.drain()
                dve.tensor_tensor(gs[:], gc[:, :, 0, :], gc[:, :, 1, :], ALU.add)
                dve.drain()
                dve.tensor_tensor(gs[:], gs[:], gc[:, :, 2, :], ALU.add)
                dve.drain()
                grouped = lsh[:].rearrange("p r (g e) -> p r g e", g=NGRP)
                dve.tensor_tensor(grouped, grouped, gs[:].unsqueeze(3).to_broadcast([P, CT, NGRP, E // NGRP]), ALU.mult)
                dve.drain()
                for r in range(CT):
                    dve.max(w8[:, r, :], lsh[:, r, :])
                dve.drain()
                for r in range(CT):
                    dve.max_index(ei[:, r, :], w8[:, r, :], lsh[:, r, :])
                dve.tensor_copy(WK[:, bass.ds(c * CT, CT), :], w8[:, :, 0:TOPK])
                dve.drain()
                dve.tensor_copy(eif[:], ei[:])
                shared(2)
                dve.drain()
                dve.tensor_tensor(OH[:], iota.unsqueeze(1).unsqueeze(1).to_broadcast([P, CT, TOPK, E]),
                                  eif[:, :, 0:TOPK].unsqueeze(3).to_broadcast([P, CT, TOPK, E]), ALU.is_equal)
                dve.drain()
                dve.tensor_reduce(sel[:], OH[:].rearrange("p r k e -> p r e k"), AX.X, ALU.add)
                dve.drain()
                dve.wait_ge(place_psum, k + 1)
                dve.wait_ge(last_psum, k + 1)
                dve.tensor_copy(selb[:], sel[:])
                dve.tensor_tensor(selt[:], sel[:], consts[:, bass.ds(c * CT + where["tok"][0], CT)].unsqueeze(2).to_broadcast([P, CT, E]),
                                  ALU.mult).then_inc(sel_ready, 1)
                shared(3)
                dve.wait_ge(shared_out, k + 1 + 1)
                for i, b in ((0, 7), (1, 3)):
                    xc = X[:, bass.ds(c * CT + 2 * i, 2), :]
                    dve.tensor_tensor(xc, xc, PS[:, b, :].rearrange("p (r n) -> p r n", r=2), ALU.add)
                dve.wait_ge(place_psum, k + 1 + 1)
                dve.tensor_tensor(slot[:], PS[:, 4, 0:CT * E].rearrange("p (r e) -> p r e", r=CT), bcast(run[:], 1, [P, CT, E]), ALU.add)
                dve.drain()
                dve.tensor_tensor(run[:], run[:], PS[:, 4, CT * E:(CT + 1) * E], ALU.add)
                dve.tensor_scalar(over[:], slot[:], CAP - 1.5, OVER, ALU.is_ge, ALU.mult)
                dve.drain()
                dve.scalar_tensor_tensor(slot[:].rearrange("p r e -> p r e"), slot[:], CAP - 1.0, over[:], ALU.min, ALU.add)
                dve.drain()
                dve.tensor_scalar(eb[par][:], eif[:, :, 0:TOPK], float(CAP), None, ALU.mult)
                dve.tensor_tensor(OH[:], OH[:], bcast(slot[:], 2, [P, CT, TOPK, E]), ALU.mult)
                dve.drain()
                dve.tensor_reduce(sl[par][:], OH[:], AX.X, ALU.add)
                dve.drain()
                dve.tensor_scalar(sc_[:], sl[par][:], OVER, -OVER, ALU.is_ge, ALU.mult)
                dve.drain()
                dve.tensor_tensor(sc_[:], sc_[:], eb[par][:], ALU.add)
                dve.drain()
                dve.tensor_tensor(CIDX[:, bass.ds(c * CT, CT), :], sl[par][:], sc_[:], ALU.add)
                dve.wait_ge(last_psum, k + 1 + 1)
                dve.tensor_reduce(runlast[:, 1:2], PS[0:E, 5, :], AX.X, ALU.max)
                dve.drain()
                dve.tensor_tensor(runlast[:, 0:1], runlast[:, 0:1], runlast[:, 1:2], ALU.max).then_inc(routed, 1)
                dve.drain()

            def start_counts():
                dve.memset(run[:], 0.0)
                dve.memset(runlast[:], 0.0)
                dve.drain()

            def last_tokens():
                dve.tensor_scalar(lidx[:], runlast[:, 0:1], -1.0, 0.0, ALU.add, ALU.max).then_inc(last_index, 1)

            def experts(f):
                with dve.Fori(0, E // EU) as ee:
                    K = ee * EU + E * f
                    for q in range(EU):
                        dve.wait_ge(gate_tanh, K + q + 1)
                        dve.wait_ge(down_psum, K + max(0, q - 1) + 1)
                        bank = PS[0:MH, 4 + q % 2, :]
                        dve.scalar_tensor_tensor(gta[:], gth[:, q % 2, :], 1.0, bank[:, 0:2 * CAP], ALU.add, ALU.mult)
                        dve.drain()
                        dve.scalar_tensor_tensor(ha[:, q % 2, :, :].rearrange("p m s -> p (m s)"), bank[:, 2 * CAP:4 * CAP], 0.5,
                                                 gta[:], ALU.mult, ALU.mult).then_inc(act_ready, 1)
                        dve.drain()

            def combine(f, c):
                for r in range(CT):
                    dve.wait_ge(gathered[r], c * (16 * TOPK) + 16 * TOPK * (NC * f + 1))
                    xt = X[:, c * CT + r, :]
                    for j in range(TOPK):
                        last = dve.scalar_tensor_tensor(xt, GB[:, r, j, :], WK[:, c * CT + r, j:j + 1], xt, ALU.mult, ALU.add)
                        if j < TOPK - 1:
                            dve.drain()
                    last.then_inc(combined, 1)
                dve.drain()

            def recur(c):
                n = n_rec(c)
                norm_chunk(dve, n, c, xr)
                dve.wait_ge(decay_ready, c + 1)
                dve.tensor_tensor(qa_[:], ra_[:], ra_[:], ALU.mult).then_inc(square_ready, 1)
                dve.scalar_tensor_tensor(ia_[:], ia_[:], 1.0, xnT[:], ALU.add, ALU.mult).then_inc(input_ready, 1)
                dve.drain()
                dve.wait_ge(root_ready, c + 1)
                dve.scalar_tensor_tensor(ia_[:], qa_[:], 0.5, ia_[:], ALU.mult, ALU.mult)
                dve.drain()
                for h in range(CH):
                    last = dve.tensor_tensor_scan(hT[:, h, :], ra_[:, h, :], ia_[:, h, :], hc[:, h:h + 1], ALU.mult, ALU.add)
                last.then_inc(state_ready, 1)
                dve.drain()
                dve.tensor_copy(hc[:], hT[:, :, CW - 1])
                dve.wait_ge(state_psum, c + 1)
                xc = X[:, bass.ds(c * CT, CT), :].rearrange("p r n -> p (r n)")
                dve.tensor_tensor(xc, xc, PS[:, 6:8, :].rearrange("p b n -> p (b n)"), ALU.add).then_inc(x3_ready, 1)
                dve.drain()

            start_counts()
            with dve.Fori(0, NC // 2) as cc:
                for par in range(2):
                    route(0, cc * 2 + par, par, cc)
            last_tokens()
            experts(0)
            start_counts()
            with dve.Fori(0, NC // 2) as cc:
                for par in range(2):
                    c = cc * 2 + par
                    combine(0, c)
                    recur(c)
                    route(1, c, par, cc)
            last_tokens()
            experts(1)
            with dve.Fori(0, NC) as c:
                combine(1, c)


def kernel(**inputs):
    import concourse.bacc as bacc
    from concourse.bass_utils import run_bass_kernel_spmd as launch

    def arr(name):
        return np.asarray(inputs["L0_" + name])

    def halves(w):
        return np.ascontiguousarray(w.T.reshape(CH, P, -1).transpose(1, 0, 2))

    table, where, cs = constants()
    Wg, Wu, Wd = arr("ffn_Wg"), arr("ffn_Wu"), arr("ffn_Wd")
    laid = [
        ("x", arr("attn_a_x")[0]),
        ("wqkv", halves(np.concatenate([arr("attn_a_Wq"), arr("attn_a_Wk"), arr("attn_a_Wv")], 0))),
        ("wo", arr("attn_a_Wo").T.reshape(G, HG, D, C).transpose(2, 1, 0, 3)),
        ("bo", arr("attn_a_bo").reshape(1, C)),
        ("nw", np.broadcast_to(np.stack([arr("attn_a_q_norm_w"), arr("attn_a_k_norm_w")]), (P, 2, D))),
        ("gate", halves(arr("ffn_gate_weight"))),
        ("wgu", np.concatenate([Wg, Wu], 1).transpose(0, 2, 1).reshape(E, CH, P, 2 * M).transpose(0, 2, 1, 3)),
        ("wd", Wd.transpose(0, 2, 1).reshape(E, 2, MH, C).transpose(0, 2, 1, 3)),
        ("sgu", halves(np.concatenate([arr("ffn_Sg"), arr("ffn_Su")], 0))),
        ("sd", arr("ffn_Sd").T.reshape(SC, MH, C).transpose(1, 0, 2)),
        ("wab", halves(np.concatenate([arr("attn_b_Wa"), arr("attn_b_Wx")], 0))),
        ("bab", np.stack([arr("attn_b_ba"), arr("attn_b_bx"), arr("attn_b_Lam")]).reshape(3, CH, P).transpose(2, 0, 1)),
        ("table", table),
        ("cs", cs),
    ]
    nc = bacc.Bacc("TRN2", target_bir_lowering=False, num_devices=1)
    arrays, args = {}, []
    for name, a in laid:
        arrays[f"in_{name}"] = a = np.ascontiguousarray(a)
        args.append(nc.dram_tensor(f"in_{name}", a.shape, mybir.dt.from_np(a.dtype), kind="ExternalInput").ap())
    args.append(nc.dram_tensor("out", (T, C), F32, kind="ExternalOutput").ap())
    hybrid_kernel(nc, *args, where)
    r = launch(nc, [arrays], core_ids=[0])
    return r.results[0]["out"].reshape(1, T, C)
```
